# Optimizing a Trainium2 kernel written in Bass

```python
import numpy as np
import jax
import jax.numpy as jnp

def _softmax(x, axis=-1):
    return jax.nn.softmax(x, axis=axis)

def _gelu(x):
    return jax.nn.gelu(x, approximate=True)

def _silu(x):
    return jax.nn.silu(x)

def _sigmoid(x):
    return jax.nn.sigmoid(x)

def _layernorm(x, axis=-1, eps=1e-05):
    m = jnp.mean(x, axis=axis, keepdims=True)
    v = jnp.var(x, axis=axis, keepdims=True)
    return (x - m) / jnp.sqrt(v + eps)

def _scatter_add(tgt, idx, src, axis=0):
    return tgt.at[idx].add(src)

def _segment_sum(src, seg, n):
    return jax.ops.segment_sum(src, seg, n)
kernel_name = 'mk_rec_standalone_d1_rec_r8_c1be69'

def setup_inputs(seed: int=0):
    np.random.seed(seed)
    _w = jnp.asarray

    def _rec_inputs():
        import jax
        import jax.numpy as jnp
        _rk = jax.random.key(seed)
        r_logits = -0.00608245 + 1.00131 * jax.random.normal(jax.random.fold_in(_rk, 1), (512, 64), jnp.float32)
        r_y_true = jax.random.bernoulli(jax.random.fold_in(_rk, 2), 0.01, (512, 100)).astype(jnp.float32)
        return (r_logits, r_y_true)
    r_logits, r_y_true = _rec_inputs()

    def _L0_rec_setup():
        import jax, jax.numpy as jnp
        import numpy as np
        SPLIT_SHAPE = (16, 16, 16, 16)
        NUM_CLASSES = 100
        STABLE = 1e-06
        key = jax.random.key(seed)
        k1, k2 = jax.random.split(key)
        B = 1024
        logits = jax.random.normal(k1, (B, sum(SPLIT_SHAPE)), dtype=jnp.float32)
        labels = jax.random.randint(k2, (B,), 0, NUM_CLASSES)
        y_true = jax.nn.one_hot(labels, NUM_CLASSES, dtype=jnp.float32)
        return {'logits': logits, 'y_true': y_true}
    _L0_rec_all = _L0_rec_setup()
    _L0_rec_in = {k: v for k, v in _L0_rec_all.items() if k in ()}
    del _L0_rec_all
    return {'r_logits': r_logits, 'r_y_true': r_y_true}

def reference(r_logits, r_y_true):
    import jax
    import jax.numpy as jnp

    def _L0_rec_ref(logits, y_true):
        import jax, jax.numpy as jnp
        import numpy as np
        SPLIT_SHAPE = (16, 16, 16, 16)
        NUM_CLASSES = 100
        STABLE = 1e-06
        B = logits.shape[0]
        splits = np.cumsum(SPLIT_SHAPE)[:-1]
        variables = [jax.nn.softmax(p, axis=-1) for p in jnp.split(logits, splits, axis=-1)]
        joint = variables[0]
        for v in variables[1:]:
            joint = jnp.einsum('b...,ba->b...a', joint, v)
        flat = joint.reshape(B, -1)
        num_y_joint = jnp.einsum('bj,by->yj', flat, y_true)
        num_joint = jnp.sum(flat, axis=0)
        prob_y_joint = jnp.clip(jnp.maximum(num_y_joint, STABLE) / jnp.maximum(num_joint, STABLE), 0.0, 1.0)
        probs = jnp.einsum('yj,bj->by', prob_y_joint, flat)
        return probs
    y = _L0_rec_ref(r_logits, r_y_true)
    return y

_drawn_inputs = setup_inputs


def setup_inputs(seed=0):
    import zlib

    import numpy as np

    out = dict(_drawn_inputs(seed))
    spreads = {}
    factors = {}
    for name, (base, spread) in spreads.items():
        noise = np.random.default_rng([zlib.crc32(name.encode()), seed]).standard_normal(out[name].shape)
        drawn = base * np.exp(spread * noise) if base else spread * noise
        out[name] = jnp.asarray(drawn.astype(out[name].dtype))
    for name, factor in factors.items():
        out[name] = (out[name] * factor).astype(out[name].dtype)
    return out
```

```python
import concourse.bass as bass
import numpy as np
from concourse import mybir
from contextlib import ExitStack

FP32 = mybir.dt.float32
FP16 = mybir.dt.float16
ALU = mybir.AluOpType
ACT = mybir.ActivationFunctionType
AX = mybir.AxisListType


def joint_classifier(nc: bass.Bass, logits: bass.AP, y_true: bass.AP, probs: bass.AP):
    ROWS, WIDTH = logits.shape
    CLASSES = y_true.shape[1]
    LANES = 128
    KC = ROWS // LANES
    S = 16
    NV = WIDTH // S
    AG = 4
    GROUPS = S // AG
    HALF = S * S // 2
    TILES = S * 2
    CW = CLASSES + 1
    NW = AG * CW
    PW = AG * CLASSES
    TW = ROWS
    QW = KC * NW
    assert HALF == LANES and NV == 4 and KC * LANES == ROWS

    UP = 2.0 ** 15
    STABLE = float(np.float32(1e-6)) * UP * UP

    ctx = ExitStack()
    with ctx:
        def sb(name, shape, dt):
            return ctx.enter_context(nc.sbuf_tensor(name, shape, dt))

        def pb(name, shape, dt):
            return ctx.enter_context(nc.psum_tensor(name, shape, dt))

        def sem(name):
            return ctx.enter_context(nc.semaphore(name))

        v1_dram = nc.dram_tensor("v1_rows", [S, ROWS], FP32, kind="Internal").ap()

        x = sb("x", [LANES, KC * NV, S], FP32)
        v = sb("v", [LANES, KC * NV, S], FP32)
        stat = sb("stat", [LANES, 2, KC * NV], FP32)
        v0f = sb("v0f", [LANES, KC, S], FP32)
        labels = sb("labels", [LANES, KC, CW], FP32)
        ident = sb("ident", [LANES, LANES], FP32)
        p23 = sb("p23", [LANES, KC, 2 * HALF], FP32)
        p23t = sb("p23t", [LANES, 2, ROWS], FP32)
        v1t = sb("v1t", [S, ROWS], FP32)
        V1_BUFS = 4
        v1b = sb("v1b", [LANES, V1_BUFS, ROWS], FP32)
        ptf = sb("ptf", [LANES, 2, ROWS], FP32)
        p_hi = sb("p_hi", [LANES, TILES * TW], FP16)
        p_lo = sb("p_lo", [LANES, TILES * TW], FP16)
        pt_hi = sb("pt_hi", [LANES, TILES * TW], FP16)
        pt_lo = sb("pt_lo", [LANES, TILES * TW], FP16)
        q_hi = sb("q_hi", [LANES, GROUPS * QW], FP16)
        q_lo = sb("q_lo", [LANES, GROUPS * QW], FP16)
        qf = sb("qf", [LANES, QW], FP32)
        qg = sb("qg", [LANES, QW], FP32)
        den = sb("den", [LANES, 2, AG], FP32)
        inv = sb("inv", [LANES, 2, AG], FP32)
        ratio = sb("ratio", [LANES, 2, PW], FP32)
        r_hi = sb("r_hi", [LANES, 2, PW], FP16)
        r_lo = sb("r_lo", [LANES, 2, PW], FP16)
        acc = sb("acc", [LANES, KC, CLASSES], FP32)

        numbers = [pb(f"numbers{i}", [LANES, 512], FP32) for i in range(2)]
        joined = [pb(f"joined{i}", [LANES, 512], FP32) for i in range(KC)]
        turned = [pb(f"turned{i}", [LANES, 512], FP32) for i in range(2)]

        logits_in = sem("logits_in")
        labels_in = sem("labels_in")
        ones_set = sem("ones_set")
        ident_set = sem("ident_set")
        acc_set = sem("acc_set")
        dve_chain = sem("dve_chain")
        shifted = sem("shifted")
        exps = sem("exps")
        soft = sem("soft")
        v1_turned = sem("v1_turned")
        v1_copied = sem("v1_copied")
        v1_stored = sem("v1_stored")
        v1_spread = [sem(f"v1_spread{i}") for i in range(V1_BUFS)]
        p23_made = sem("p23_made")
        p23_turned = sem("p23_turned")
        p23t_made = sem("p23t_made")
        q0_made = sem("q0_made")
        q0_hi = sem("q0_hi")
        q_ready = sem("q_ready")
        pool_chain = sem("pool_chain")
        v0f_made = sem("v0f_made")
        p_hi_made = sem("p_hi_made")
        p_ready = sem("p_ready")
        ptf_made = sem("ptf_made")
        pt_hi_made = sem("pt_hi_made")
        pt_ready = sem("pt_ready")
        numbers_ready = sem("numbers_ready")
        den_made = sem("den_made")
        inv_made = sem("inv_made")
        ratio_made = sem("ratio_made")
        r_hi_made = sem("r_hi_made")
        ratios_ready = sem("ratios_ready")
        joined_ready = sem("joined_ready")
        added = sem("added")
        stored = sem("stored")

        block = ctx.enter_context(nc.Block())

        @block.sync
        def _(sp):
            sp.dma_start(x[:, :, :], logits.rearrange("(p k) (v s) -> p (k v) s", k=KC, s=S)).then_inc(logits_in, 16)
            sp.wait_ge(v1_copied, 1)
            sp.dma_start(v1_dram, v1t[:, :]).then_inc(v1_stored, 16)
            sp.wait_ge(v1_stored, 16)
            for i in range(V1_BUFS):
                sp.dma_start(v1b[:, i, :], v1_dram[i:i + 1, :].broadcast_to([LANES, ROWS])).then_inc(v1_spread[i], 16)
            with sp.Fori(V1_BUFS, S - V1_BUFS + 1, V1_BUFS) as i:
                for j in range(V1_BUFS):
                    sp.wait_ge(ptf_made, 2 * i + 2 * (j + 1 - V1_BUFS))
                    sp.dma_start(v1b[:, j, :],
                                 v1_dram[bass.ds(i + j, 1), :].broadcast_to([LANES, ROWS])).then_inc(v1_spread[j], 16)
            out = probs.rearrange("(p k) y -> p k y", k=KC)
            sp.wait_ge(added, GROUPS * KC * AG)
            sp.dma_start(out, acc[:, :, :]).then_inc(stored, 16)
            sp.wait_ge(stored, 16)

        @block.gpsimd
        def _(pool):
            pool.memset(labels[:, :, CLASSES:CW], 1.0).then_inc(ones_set, 1)
            pool.memset(ident[:, :], 0.0).then_inc(ident_set, 1)
            pool.wait_ge(ident_set, 1)
            pool.affine_select(out=ident[:, :], in_=ident[:, :], compare_op=ALU.not_equal, fill=1.0, base=0,
                               pattern=[[-1, LANES]], channel_multiplier=1).then_inc(ident_set, 1)
            pool.memset(acc[:, :, :], 0.0).then_inc(acc_set, 1)
            pool.wait_ge(soft, 1)
            vk = v[:, :, :].rearrange("p (k v) s -> p k v s", v=NV)
            pool.tensor_scalar(v0f[:, :, :], vk[:, :, 0, :], 1.0 / UP ** 3, None, ALU.mult).then_inc(v0f_made, 1)
            pool.wait_ge(labels_in, 16)
            with pool.Fori(1, GROUPS) as g:
                q4 = qg[:, :].rearrange("p (k a y) -> p k a y", k=KC, a=AG)
                v0g = vk[:, :, 0, bass.ds(AG * g, AG)].unsqueeze(3).broadcast_to([LANES, KC, AG, CW])
                yg = labels[:, :, :].unsqueeze(2).broadcast_to([LANES, KC, AG, CW])
                pool.tensor_tensor(q4, v0g, yg, ALU.mult).then_inc(pool_chain, 1)
                pool.wait_ge(pool_chain, 2 * g - 1)
                pool.tensor_copy(q_hi[:, bass.ds(QW * g, QW)], qg[:, :]).then_inc(pool_chain, 1)
                pool.wait_ge(pool_chain, 2 * g)
                pool.tensor_tensor(q_lo[:, bass.ds(QW * g, QW)], qg[:, :], q_hi[:, bass.ds(QW * g, QW)],
                                   ALU.subtract).then_inc(q_ready, 1)
                pool.wait_ge(q_ready, g + 1)

        @block.scalar
        def _(act):
            act.dma_start(labels[:, :, 0:CLASSES], y_true.rearrange("(p k) y -> p k y", k=KC)).then_inc(labels_in, 16)
            act.wait_ge(shifted, 1)
            act.activation(x[:, :, :], x[:, :, :], ACT.Exp).then_inc(exps, 1)
            act.wait_ge(v1_turned, 1)
            act.activation(v1t[:, :], numbers[1][0:S, 0:ROWS], ACT.Copy).then_inc(v1_copied, 1)

            def make_p_hi(i):
                for k in range(KC):
                    o = p_hi[:, bass.ds(i * (2 * TW), 2 * TW)].rearrange("p (h k n) -> p h k n", h=2, k=KC)
                    last = act.activation(o[:, :, k, :], p23[:, k, :].rearrange("p (h n) -> p h n", h=2), ACT.Copy,
                                          scale=v[:, k * NV + 1, bass.ds(i, 1)])
                last.then_inc(p_hi_made, 1)

            def make_pt_hi(tile, parity):
                act.wait_ge(ptf_made, tile + 1)
                act.activation(pt_hi[:, bass.ds(tile * TW, TW)], ptf[:, parity, :], ACT.Copy).then_inc(pt_hi_made, 1)

            act.wait_ge(p23_made, 1)
            make_p_hi(0)
            act.wait_ge(q0_made, 1)
            act.activation(q_hi[:, 0:QW], qf[:, :], ACT.Copy).then_inc(q0_hi, 1)
            for h in range(2):
                act.wait_ge(p23_turned, h + 1)
                act.activation(p23t[:, h, :], turned[h][:, 0:ROWS], ACT.Copy).then_inc(p23t_made, 1)
            make_pt_hi(0, 0)
            make_pt_hi(1, 1)
            with act.Fori(1, S) as i:
                make_p_hi(i)
                make_pt_hi(2 * i, 0)
                make_pt_hi(2 * i + 1, 1)

        @block.vector
        def _(dve):
            dve.wait_ge(logits_in, 16)
            dve.tensor_reduce(stat[:, 0, :], x[:, :, :], AX.X, ALU.max).then_inc(dve_chain, 1)
            dve.wait_ge(dve_chain, 1)
            dve.tensor_tensor(x[:, :, :], x[:, :, :], stat[:, 0, :].unsqueeze(2).broadcast_to([LANES, KC * NV, S]),
                              ALU.subtract).then_inc(shifted, 1)
            dve.wait_ge(exps, 1)
            dve.tensor_reduce(stat[:, 0, :], x[:, :, :], AX.X, ALU.add).then_inc(dve_chain, 1)
            dve.wait_ge(dve_chain, 2)
            dve.reciprocal(stat[:, 1, :], stat[:, 0, :]).then_inc(dve_chain, 1)
            dve.wait_ge(dve_chain, 3)
            outer = stat[:, 1, :].rearrange("p (k v) -> p k v", v=NV)[:, :, 0:NV:NV - 1]
            dve.tensor_scalar(outer, outer, UP, None, ALU.mult).then_inc(dve_chain, 1)
            dve.wait_ge(dve_chain, 4)
            dve.tensor_tensor(v[:, :, :], x[:, :, :], stat[:, 1, :].unsqueeze(2).broadcast_to([LANES, KC * NV, S]),
                              ALU.mult).then_inc(soft, 1)
            dve.wait_ge(soft, 1)
            vk = v[:, :, :].rearrange("p (k v) s -> p k v s", v=NV)
            dve.tensor_tensor(p23[:, :, :].rearrange("p k (c d) -> p k c d", c=S),
                              vk[:, :, 2, :].unsqueeze(3).broadcast_to([LANES, KC, S, S]),
                              vk[:, :, 3, :].unsqueeze(2).broadcast_to([LANES, KC, S, S]), ALU.mult).then_inc(p23_made, 1)
            dve.wait_ge(labels_in, 16)
            dve.wait_ge(ones_set, 1)
            dve.tensor_tensor(qf[:, :].rearrange("p (k a y) -> p k a y", k=KC, a=AG),
                              vk[:, :, 0, 0:AG].unsqueeze(3).broadcast_to([LANES, KC, AG, CW]),
                              labels[:, :, :].unsqueeze(2).broadcast_to([LANES, KC, AG, CW]), ALU.mult).then_inc(q0_made, 1)

            def make_p_lo(i):
                dve.wait_ge(p_hi_made, i + 1)
                for k in range(KC):
                    hi = p_hi[:, bass.ds(i * (2 * TW), 2 * TW)].rearrange("p (h k n) -> p h k n", h=2, k=KC)
                    lo = p_lo[:, bass.ds(i * (2 * TW), 2 * TW)].rearrange("p (h k n) -> p h k n", h=2, k=KC)
                    last = dve.scalar_tensor_tensor(lo[:, :, k, :], p23[:, k, :].rearrange("p (h n) -> p h n", h=2),
                                                    v[:, k * NV + 1, bass.ds(i, 1)], hi[:, :, k, :],
                                                    ALU.mult, ALU.subtract)
                last.then_inc(p_ready, 1)

            def make_ptf(buf, parity):
                dve.tensor_tensor(ptf[:, parity, :], p23t[:, parity, :], v1b[:, buf, :], ALU.mult).then_inc(ptf_made, 1)

            def make_pt_lo(tile, parity):
                dve.wait_ge(pt_hi_made, tile + 1)
                dve.tensor_tensor(pt_lo[:, bass.ds(tile * TW, TW)], ptf[:, parity, :],
                                  pt_hi[:, bass.ds(tile * TW, TW)], ALU.subtract).then_inc(pt_ready, 1)

            def make_ratios(step, parity):
                dve.wait_ge(numbers_ready, step + 1)
                got = numbers[parity][:, 0:NW].rearrange("p (a y) -> p a y", a=AG)
                dve.tensor_scalar(den[:, parity, :], got[:, :, CLASSES], STABLE, 1.0 / UP, ALU.max,
                                  ALU.mult).then_inc(den_made, 1)
                dve.wait_ge(den_made, step + 1)
                dve.reciprocal(inv[:, parity, :], den[:, parity, :]).then_inc(inv_made, 1)
                dve.wait_ge(inv_made, step + 1)
                dve.scalar_tensor_tensor(ratio[:, parity, :].rearrange("p (a y) -> p a y", a=AG),
                                         got[:, :, 0:CLASSES], STABLE,
                                         inv[:, parity, :].unsqueeze(2).broadcast_to([LANES, AG, CLASSES]),
                                         ALU.max, ALU.mult).then_inc(ratio_made, 1)
                dve.wait_ge(ratio_made, step + 1)
                dve.tensor_scalar(r_hi[:, parity, :], ratio[:, parity, :], UP, 0.0, ALU.min, ALU.max).then_inc(r_hi_made, 1)
                dve.wait_ge(r_hi_made, step + 1)
                dve.scalar_tensor_tensor(r_lo[:, parity, :], ratio[:, parity, :], UP, r_hi[:, parity, :],
                                         ALU.min, ALU.subtract).then_inc(ratios_ready, 1)

            def add_group(g):
                for k in range(KC):
                    dve.wait_ge(joined_ready, g * KC + (k + 1))
                    for a in range(AG):
                        if k or a:
                            dve.wait_ge(added, g * (KC * AG) + (k * AG + a))
                        dve.scalar_tensor_tensor(acc[:, k, :], joined[k][:, a * CLASSES:(a + 1) * CLASSES],
                                                 v0f[:, k, bass.ds(g * AG + a, 1)], acc[:, k, :],
                                                 ALU.mult, ALU.add).then_inc(added, 1)

            dve.wait_ge(q0_hi, 1)
            dve.tensor_tensor(q_lo[:, 0:QW], qf[:, :], q_hi[:, 0:QW], ALU.subtract).then_inc(q_ready, 1)
            make_p_lo(0)
            for h in range(2):
                dve.wait_ge(p23t_made, h + 1)
                if h == 0:
                    dve.wait_ge(v1_spread[0], 16)
                make_ptf(0, h)
                make_pt_lo(h, h)

            def make_next(i, buf, fill):
                make_p_lo(i)
                dve.wait_ge(v1_spread[buf], fill)
                make_ptf(buf, 0)
                make_ratios(2 * i - 2, 0)
                make_pt_lo(2 * i, 0)
                make_ptf(buf, 1)
                make_ratios(2 * i - 1, 1)
                make_pt_lo(2 * i + 1, 1)

            for i in range(1, V1_BUFS):
                make_next(i, i, 16)
            with dve.Fori(V1_BUFS, S - V1_BUFS + 1, V1_BUFS) as i:
                for j in range(V1_BUFS):
                    make_next(i + j, j, (i + V1_BUFS) * (16 // V1_BUFS))
            make_ratios(TILES - 2, 0)
            make_ratios(TILES - 1, 1)
            dve.wait_ge(v0f_made, 1)
            dve.wait_ge(acc_set, 1)
            with dve.Fori(1, GROUPS) as g:
                make_ratios(g * TILES, 0)
                add_group(g - 1)
                make_ratios(g * TILES + 1, 1)
                with dve.Fori(2, TILES - 1, 2) as t:
                    make_ratios(g * TILES + t, 0)
                    make_ratios(g * TILES + t + 1, 1)
            add_group(GROUPS - 1)

        @block.tensor
        def _(pe):
            vk = v[:, :, :].rearrange("p (k v) s -> p k v s", v=NV)
            pe.wait_ge(ident_set, 2)
            pe.wait_ge(soft, 1)
            for k in range(KC):
                last = pe.transpose(numbers[1][0:S, k * LANES:(k + 1) * LANES], vk[:, k, 1, :], ident[:, :])
            last.then_inc(v1_turned, 1)
            pe.wait_ge(p23_made, 1)
            for h in range(2):
                for k in range(KC):
                    last = pe.transpose(turned[h][:, k * LANES:(k + 1) * LANES],
                                        p23[:, k, h * HALF:(h + 1) * HALF], ident[:, :])
                last.then_inc(p23_turned, 1)

            def count(g, tile, parity):
                for k in range(KC):
                    hi = p_hi[:, bass.ds(tile * TW + k * LANES, LANES)]
                    lo = p_lo[:, bass.ds(tile * TW + k * LANES, LANES)]
                    qh = q_hi[:, bass.ds(g * QW + k * NW, NW)]
                    ql = q_lo[:, bass.ds(g * QW + k * NW, NW)]
                    out = numbers[parity][:, 0:NW]
                    pe.matmul(out, hi, qh, start=(k == 0), stop=False)
                    pe.matmul(out, hi, ql, start=False, stop=False)
                    last = pe.matmul(out, lo, qh, start=False, stop=(k == KC - 1))
                last.then_inc(numbers_ready, 1)

            def join(g, tile, parity, first=False, final=False, freed=None):
                pe.wait_ge(ratios_ready, g * TILES + tile + 1)
                for k in range(KC):
                    hi = pt_hi[:, bass.ds(tile * TW + k * LANES, LANES)]
                    lo = pt_lo[:, bass.ds(tile * TW + k * LANES, LANES)]
                    out = joined[k][:, 0:PW]
                    if freed is not None:
                        pe.wait_ge(added, freed + (k + 1) * AG)
                    pe.matmul(out, hi, r_hi[:, parity, :], start=first, stop=False)
                    pe.matmul(out, hi, r_lo[:, parity, :], start=False, stop=False)
                    last = pe.matmul(out, lo, r_hi[:, parity, :], start=False, stop=final)
                    if final:
                        last.then_inc(joined_ready, 1)

            pe.wait_ge(q_ready, 1)
            pe.wait_ge(p_ready, 1)
            count(0, 0, 0)
            pe.wait_ge(v1_copied, 1)
            count(0, 1, 1)
            pe.wait_ge(pt_ready, 1)
            join(0, 0, 0, first=True)

            def middle(g, make):
                with pe.Fori(1, S) as i:
                    if make:
                        pe.wait_ge(p_ready, i + 1)
                    count(g, 2 * i, 0)
                    if make:
                        pe.wait_ge(pt_ready, 2 * i)
                    join(g, 2 * i - 1, 1)
                    count(g, 2 * i + 1, 1)
                    if make:
                        pe.wait_ge(pt_ready, 2 * i + 1)
                    join(g, 2 * i, 0)

            middle(0, True)
            pe.wait_ge(pt_ready, TILES)
            with pe.Fori(1, GROUPS) as g:
                pe.wait_ge(q_ready, g + 1)
                count(g, 0, 0)
                join(g - 1, TILES - 1, 1, final=True)
                count(g, 1, 1)
                join(g, 0, 0, first=True, freed=(g - 1) * (KC * AG))
                middle(g, False)
            join(GROUPS - 1, TILES - 1, 1, final=True)


_INS = ["r_logits", "r_y_true"]
_OUTS = [((512, 100), "float32")]


def kernel(**inputs):
    import numpy as _np
    import concourse.bacc as _bacc
    from concourse import mybir as _mybir
    from concourse.bass_utils import run_bass_kernel_spmd as _run

    nc = _bacc.Bacc("TRN2", target_bir_lowering=False, num_devices=1)
    arrays, args = {}, []
    for name in _INS:
        a = _np.ascontiguousarray(inputs[name])
        arrays[f"in_{name}_dram"] = a
        args.append(nc.dram_tensor(f"in_{name}_dram", a.shape, _mybir.dt.from_np(a.dtype), kind="ExternalInput").ap())
    for i, (shape, dtype) in enumerate(_OUTS):
        dt = _mybir.dt.from_np(_np.dtype(dtype))
        args.append(nc.dram_tensor(f"out_{i}_dram", shape, dt, kind="ExternalOutput").ap())
    joint_classifier(nc, *args)
    r = _run(nc, [arrays], core_ids=[0])
    return r.results[0]["out_0_dram"]
```

```python
import concourse.bass as bass
import numpy as np
from concourse import mybir
from contextlib import ExitStack

FP32 = mybir.dt.float32
FP16 = mybir.dt.float16
ALU = mybir.AluOpType
ACT = mybir.ActivationFunctionType
AX = mybir.AxisListType


def joint_classifier(nc: bass.Bass, logits: bass.AP, y_true: bass.AP, probs: bass.AP):
    ROWS, WIDTH = logits.shape
    CLASSES = y_true.shape[1]
    LANES = 128
    KC = ROWS // LANES
    S = 16
    NV = WIDTH // S
    AG = 4
    GROUPS = S // AG
    HALF = S * S // 2
    TILES = S * 2
    CW = CLASSES + 1
    NW = AG * CW
    PW = AG * CLASSES
    TW = ROWS
    QW = KC * NW
    QH = QW // 2
    assert HALF == LANES and NV == 4 and KC * LANES == ROWS

    UP = 2.0 ** 15
    STABLE = float(np.float32(1e-6)) * UP * UP

    ctx = ExitStack()
    with ctx:
        def sb(name, shape, dt):
            return ctx.enter_context(nc.sbuf_tensor(name, shape, dt))

        def pb(name, shape, dt):
            return ctx.enter_context(nc.psum_tensor(name, shape, dt))

        def sem(name):
            return ctx.enter_context(nc.semaphore(name))

        v1_dram = nc.dram_tensor("v1_rows", [S, ROWS], FP32, kind="Internal").ap()

        x = sb("x", [LANES, KC * NV, S], FP32)
        v = sb("v", [LANES, KC * NV, S], FP32)
        stat = sb("stat", [LANES, 2, KC * NV], FP32)
        v0f = sb("v0f", [LANES, KC, S], FP32)
        labels = sb("labels", [LANES, KC, CW], FP32)
        ident = sb("ident", [LANES, LANES], FP32)
        p23 = sb("p23", [LANES, KC, 2 * HALF], FP32)
        p23t = sb("p23t", [LANES, 2, ROWS], FP32)
        v1t = sb("v1t", [S, ROWS], FP32)
        V1_BUFS = 4
        v1b = sb("v1b", [LANES, V1_BUFS, ROWS], FP32)
        ptf = sb("ptf", [LANES, 2, ROWS], FP32)
        p_hi = sb("p_hi", [LANES, TILES * TW], FP16)
        p_lo = sb("p_lo", [LANES, TILES * TW], FP16)
        pt_hi = sb("pt_hi", [LANES, TILES * TW], FP16)
        pt_lo = sb("pt_lo", [LANES, TILES * TW], FP16)
        q_hi = sb("q_hi", [LANES, GROUPS * QW], FP16)
        q_lo = sb("q_lo", [LANES, GROUPS * QW], FP16)
        qf = sb("qf", [LANES, QW], FP32)
        qg = sb("qg", [LANES, QW], FP32)
        SLOTS = 3
        den = sb("den", [LANES, SLOTS, AG], FP32)
        inv = sb("inv", [LANES, SLOTS, AG], FP32)
        ratio = sb("ratio", [LANES, SLOTS, PW], FP32)
        r_hi = sb("r_hi", [LANES, SLOTS, PW], FP16)
        r_lo = sb("r_lo", [LANES, SLOTS, PW], FP16)
        left = qf[:, 0:KC * PW].rearrange("p (k a y) -> p k a y", k=KC, a=AG)
        part = qg[:, 0:KC * PW].rearrange("p (k a y) -> p k a y", k=KC, a=AG)
        acc = sb("acc", [LANES, KC, CLASSES], FP32)

        numbers = [pb(f"numbers{i}", [LANES, 512], FP32) for i in range(SLOTS)]
        joined = [pb(f"joined{i}", [LANES, 512], FP32) for i in range(KC)]
        spare = pb("spare", [LANES, 512], FP32)
        turned = [numbers[2], spare]
        v1_psum = joined[0]
        v1_first = joined[1]

        logits_in = sem("logits_in")
        labels_in = sem("labels_in")
        ones_set = sem("ones_set")
        ident_set = sem("ident_set")
        acc_set = sem("acc_set")
        dve_chain = sem("dve_chain")
        shifted = sem("shifted")
        exps = sem("exps")
        soft = sem("soft")
        v1_turned = sem("v1_turned")
        v1_copied = sem("v1_copied")
        v1_stored = sem("v1_stored")
        v1_first_made = sem("v1_first_made")
        v1_first_copied = sem("v1_first_copied")
        v1_spread = [sem(f"v1_spread{i}") for i in range(V1_BUFS)]
        p23_made = sem("p23_made")
        p23_turned = sem("p23_turned")
        p23t_made = sem("p23t_made")
        q0_left = sem("q0_left")
        q0_right = sem("q0_right")
        q0_right_hi = sem("q0_right_hi")
        q0_left_lo = sem("q0_left_lo")
        q0_right_lo = sem("q0_right_lo")
        q_ready = sem("q_ready")
        q_chain = sem("q_chain")
        v0f_made = sem("v0f_made")
        p_hi_made = sem("p_hi_made")
        p_ready = sem("p_ready")
        ptf_made = sem("ptf_made")
        pt_hi_made = sem("pt_hi_made")
        pt_ready = sem("pt_ready")
        numbers_ready = sem("numbers_ready")
        den_made = sem("den_made")
        inv_made = sem("inv_made")
        ratio_made = sem("ratio_made")
        r_hi_made = sem("r_hi_made")
        ratios_ready = sem("ratios_ready")
        joined_ready = sem("joined_ready")
        left_made = sem("left_made")
        sum_chain = sem("sum_chain")
        summed = sem("summed")
        added = sem("added")
        stored = sem("stored")

        vk = v[:, :, :].rearrange("p (k v) s -> p k v s", v=NV)
        block = ctx.enter_context(nc.Block())

        @block.sync
        def _(sp):
            sp.dma_start(x[:, :, :], logits.rearrange("(p k) (v s) -> p (k v) s", k=KC, s=S)).then_inc(logits_in, 16)
            sp.wait_ge(v1_copied, 1)
            sp.dma_start(v1_dram, v1t[:, :]).then_inc(v1_stored, 16)
            sp.wait_ge(v1_stored, 16)
            for i in range(1, V1_BUFS):
                sp.dma_start(v1b[:, i, :], v1_dram[i:i + 1, :].broadcast_to([LANES, ROWS])).then_inc(v1_spread[i], 16)
            sp.wait_ge(ptf_made, 2)
            sp.dma_start(v1b[:, 0, :],
                         v1_dram[V1_BUFS:V1_BUFS + 1, :].broadcast_to([LANES, ROWS])).then_inc(v1_spread[0], 16)
            def refill(i, buf):
                sp.wait_ge(ptf_made, 2 * i + 2 * (1 - V1_BUFS))
                sp.dma_start(v1b[:, buf, :],
                             v1_dram[bass.ds(i, 1), :].broadcast_to([LANES, ROWS])).then_inc(v1_spread[buf], 16)

            with sp.Fori(V1_BUFS, S - 2 * V1_BUFS + 1, V1_BUFS) as i:
                for j in range(1, V1_BUFS + 1):
                    refill(i + j, j % V1_BUFS)
            for i in range(S - V1_BUFS + 1, S):
                refill(i, i % V1_BUFS)
            sp.wait_ge(added, KC * AG)
            sp.dma_start(probs.rearrange("(p k) y -> p k y", k=KC), acc[:, :, :]).then_inc(stored, 16)
            sp.wait_ge(stored, 16)

        def v0_times_y(eng, out, k0, k1, group):
            v0g = vk[:, k0:k1, 0, bass.ds(AG * group, AG)].unsqueeze(3).broadcast_to([LANES, k1 - k0, AG, CW])
            yg = labels[:, k0:k1, :].unsqueeze(2).broadcast_to([LANES, k1 - k0, AG, CW])
            return eng.tensor_tensor(out.rearrange("p (k a y) -> p k a y", k=k1 - k0, a=AG), v0g, yg, ALU.mult)

        @block.gpsimd
        def _(pool):
            pool.memset(labels[:, :, CLASSES:CW], 1.0).then_inc(ones_set, 1)
            pool.memset(ident[:, :], 0.0).then_inc(ident_set, 1)
            pool.wait_ge(ident_set, 1)
            pool.affine_select(out=ident[:, :], in_=ident[:, :], compare_op=ALU.not_equal, fill=1.0, base=0,
                               pattern=[[-1, LANES]], channel_multiplier=1).then_inc(ident_set, 1)
            pool.memset(acc[:, :, :], 0.0).then_inc(acc_set, 1)
            pool.wait_ge(soft, 1)
            pool.wait_ge(labels_in, 16)
            pool.wait_ge(ones_set, 1)
            v0_times_y(pool, qf[:, QH:QW], KC // 2, KC, 0).then_inc(q0_right, 1)
            pool.wait_ge(q0_right_hi, 1)
            pool.tensor_tensor(q_lo[:, QH:QW], qf[:, QH:QW], q_hi[:, QH:QW], ALU.subtract).then_inc(q0_right_lo, 1)

            def make_pt(tile, half, buf, fill):
                if half == 0 and fill is not None:
                    pool.wait_ge(v1_spread[buf], fill)
                if fill is not None:
                    pool.wait_ge(pt_ready, tile - 1)
                pool.tensor_tensor(ptf[:, half, :], p23t[:, half, :], v1b[:, buf, :], ALU.mult).then_inc(ptf_made, 1)

            def finish_pt(tile, half):
                pool.wait_ge(pt_hi_made, tile + 1)
                pool.tensor_tensor(pt_lo[:, bass.ds(tile * TW, TW)], ptf[:, half, :],
                                   pt_hi[:, bass.ds(tile * TW, TW)], ALU.subtract).then_inc(pt_ready, 1)

            def make_value(i, buf, fill):
                make_pt(2 * i, 0, buf, fill)
                make_pt(2 * i + 1, 1, buf, fill)
                finish_pt(2 * i, 0)
                finish_pt(2 * i + 1, 1)

            pool.wait_ge(v1_first_copied, 1)
            pool.wait_ge(p23t_made, 1)
            make_pt(0, 0, 0, None)
            finish_pt(0, 0)
            pool.wait_ge(p23t_made, 2)
            make_pt(1, 1, 0, None)
            finish_pt(1, 1)
            for i in range(1, V1_BUFS):
                make_value(i, i, 16)
            with pool.Fori(V1_BUFS, S - V1_BUFS + 1, V1_BUFS) as i:
                make_value(i, 0, i * (16 // V1_BUFS))
                for j in range(1, V1_BUFS):
                    make_value(i + j, j, (i + V1_BUFS) * (16 // V1_BUFS))

            with pool.Fori(1, GROUPS) as g:
                v0_times_y(pool, qg[:, :], 0, KC, g).then_inc(q_chain, 1)
                pool.wait_ge(q_chain, 2 * g - 1)
                pool.tensor_copy(q_hi[:, bass.ds(QW * g, QW)], qg[:, :]).then_inc(q_chain, 1)
                pool.wait_ge(q_chain, 2 * g)
                pool.tensor_tensor(q_lo[:, bass.ds(QW * g, QW)], qg[:, :], q_hi[:, bass.ds(QW * g, QW)],
                                   ALU.subtract).then_inc(q_ready, 1)
                pool.wait_ge(q_ready, g)

            pool.tensor_scalar(v0f[:, :, :], vk[:, :, 0, :], 1.0 / UP ** 3, None, ALU.mult).then_inc(v0f_made, 1)
            pool.wait_ge(v0f_made, 1)
            pool.wait_ge(acc_set, 1)
            with pool.Fori(1, GROUPS) as g:
                pool.wait_ge(left_made, g * KC)
                pool.tensor_tensor(part[:, :, :, :], left[:, :, :, :],
                                   v0f[:, :, bass.ds((g - 1) * AG, AG)].unsqueeze(3).broadcast_to([LANES, KC, AG, CLASSES]),
                                   ALU.mult).then_inc(sum_chain, 1)
                pool.wait_ge(sum_chain, 3 * g - 2)
                pool.tensor_tensor(part[:, :, 0:2, :], part[:, :, 0:2, :], part[:, :, 2:4, :],
                                   ALU.add).then_inc(sum_chain, 1)
                pool.wait_ge(sum_chain, 3 * g - 1)
                pool.tensor_tensor(part[:, :, 0, :], part[:, :, 0, :], part[:, :, 1, :], ALU.add).then_inc(sum_chain, 1)
                pool.wait_ge(sum_chain, 3 * g)
                pool.tensor_tensor(acc[:, :, :], acc[:, :, :], part[:, :, 0, :], ALU.add).then_inc(summed, 1)
                pool.wait_ge(summed, g)

        @block.scalar
        def _(act):
            act.dma_start(labels[:, :, 0:CLASSES], y_true.rearrange("(p k) y -> p k y", k=KC)).then_inc(labels_in, 16)
            act.wait_ge(shifted, 1)
            act.activation(x[:, :, :], x[:, :, :], ACT.Exp).then_inc(exps, 1)

            def make_p_hi(i, h0, h1):
                o = p_hi[:, bass.ds(i * (2 * TW), 2 * TW)].rearrange("p (h k n) -> p h k n", h=2, k=KC)
                for k in range(KC):
                    last = act.activation(o[:, h0:h1, k, :],
                                          p23[:, k, h0 * HALF:h1 * HALF].rearrange("p (h n) -> p h n", n=HALF),
                                          ACT.Copy, scale=v[:, k * NV + 1, bass.ds(i, 1)])
                last.then_inc(p_hi_made, h1 - h0)

            def make_pt_hi(tile, half):
                act.wait_ge(ptf_made, tile + 1)
                act.activation(pt_hi[:, bass.ds(tile * TW, TW)], ptf[:, half, :], ACT.Copy).then_inc(pt_hi_made, 1)

            act.wait_ge(p23_made, 1)
            make_p_hi(0, 0, 1)
            act.wait_ge(q0_right, 1)
            act.activation(q_hi[:, QH:QW], qf[:, QH:QW], ACT.Copy).then_inc(q0_right_hi, 1)
            act.wait_ge(v1_turned, 1)
            act.activation(v1t[:, :], v1_psum[0:S, 0:ROWS], ACT.Copy).then_inc(v1_copied, 1)
            act.wait_ge(p23_made, 2)
            make_p_hi(0, 1, 2)
            act.wait_ge(v1_first_made, 1)
            act.activation(v1b[:, 0, :], v1_first[:, 0:ROWS], ACT.Copy).then_inc(v1_first_copied, 1)
            for h in range(2):
                act.wait_ge(p23_turned, h + 1)
                act.activation(p23t[:, h, :], turned[h][:, 0:ROWS], ACT.Copy).then_inc(p23t_made, 1)
            make_pt_hi(0, 0)
            with act.Fori(1, S) as i:
                make_p_hi(i, 0, 2)
                make_pt_hi(2 * i - 1, 1)
                make_pt_hi(2 * i, 0)
            make_pt_hi(TILES - 1, 1)
            with act.Fori(1, GROUPS) as g:
                for k in range(KC):
                    act.wait_ge(joined_ready, (g - 1) * KC + (k + 1))
                    act.activation(left[:, k, :, :], joined[k][:, 0:PW].rearrange("p (a y) -> p a y", a=AG),
                                   ACT.Copy).then_inc(left_made, 1)
                act.wait_ge(sum_chain, 3 * g - 2)

        @block.vector
        def _(dve):
            dve.wait_ge(logits_in, 16)
            dve.tensor_reduce(stat[:, 0, :], x[:, :, :], AX.X, ALU.max).then_inc(dve_chain, 1)
            dve.wait_ge(dve_chain, 1)
            dve.tensor_tensor(x[:, :, :], x[:, :, :], stat[:, 0, :].unsqueeze(2).broadcast_to([LANES, KC * NV, S]),
                              ALU.subtract).then_inc(shifted, 1)
            dve.wait_ge(exps, 1)
            dve.tensor_reduce(stat[:, 0, :], x[:, :, :], AX.X, ALU.add).then_inc(dve_chain, 1)
            dve.wait_ge(dve_chain, 2)
            dve.reciprocal(stat[:, 1, :], stat[:, 0, :]).then_inc(dve_chain, 1)
            dve.wait_ge(dve_chain, 3)
            outer = stat[:, 1, :].rearrange("p (k v) -> p k v", v=NV)[:, :, 0:NV:NV - 1]
            dve.tensor_scalar(outer, outer, UP, None, ALU.mult).then_inc(dve_chain, 1)
            dve.wait_ge(dve_chain, 4)
            dve.tensor_tensor(v[:, :, :], x[:, :, :], stat[:, 1, :].unsqueeze(2).broadcast_to([LANES, KC * NV, S]),
                              ALU.mult).then_inc(soft, 1)
            dve.wait_ge(soft, 1)

            def make_p23(h):
                c = S // 2
                dve.tensor_tensor(p23[:, :, h * HALF:(h + 1) * HALF].rearrange("p k (c d) -> p k c d", d=S),
                                  vk[:, :, 2, h * c:(h + 1) * c].unsqueeze(3).broadcast_to([LANES, KC, c, S]),
                                  vk[:, :, 3, :].unsqueeze(2).broadcast_to([LANES, KC, c, S]),
                                  ALU.mult).then_inc(p23_made, 1)

            def make_p_lo(i, h0, h1):
                dve.wait_ge(p_hi_made, 2 * i + h1)
                hi = p_hi[:, bass.ds(i * (2 * TW), 2 * TW)].rearrange("p (h k n) -> p h k n", h=2, k=KC)
                lo = p_lo[:, bass.ds(i * (2 * TW), 2 * TW)].rearrange("p (h k n) -> p h k n", h=2, k=KC)
                for k in range(KC):
                    last = dve.scalar_tensor_tensor(lo[:, h0:h1, k, :],
                                                    p23[:, k, h0 * HALF:h1 * HALF].rearrange("p (h n) -> p h n", n=HALF),
                                                    v[:, k * NV + 1, bass.ds(i, 1)], hi[:, h0:h1, k, :],
                                                    ALU.mult, ALU.subtract)
                last.then_inc(p_ready, h1 - h0)

            def make_ratios(step, slot):
                dve.wait_ge(numbers_ready, step + 1)
                got = numbers[slot][:, 0:NW].rearrange("p (a y) -> p a y", a=AG)
                dve.tensor_scalar(den[:, slot, :], got[:, :, CLASSES], STABLE, 1.0 / UP, ALU.max,
                                  ALU.mult).then_inc(den_made, 1)
                dve.wait_ge(den_made, step + 1)
                dve.reciprocal(inv[:, slot, :], den[:, slot, :]).then_inc(inv_made, 1)
                dve.wait_ge(inv_made, step + 1)
                dve.scalar_tensor_tensor(ratio[:, slot, :].rearrange("p (a y) -> p a y", a=AG),
                                         got[:, :, 0:CLASSES], STABLE,
                                         inv[:, slot, :].unsqueeze(2).broadcast_to([LANES, AG, CLASSES]),
                                         ALU.max, ALU.mult).then_inc(ratio_made, 1)
                dve.wait_ge(ratio_made, step + 1)
                dve.tensor_scalar(r_hi[:, slot, :], ratio[:, slot, :], UP, 0.0, ALU.min, ALU.max).then_inc(r_hi_made, 1)
                dve.wait_ge(r_hi_made, step + 1)
                dve.scalar_tensor_tensor(r_lo[:, slot, :], ratio[:, slot, :], UP, r_hi[:, slot, :],
                                         ALU.min, ALU.subtract).then_inc(ratios_ready, 1)

            make_p23(0)
            dve.wait_ge(labels_in, 16)
            dve.wait_ge(ones_set, 1)
            v0_times_y(dve, qf[:, 0:QH], 0, KC // 2, 0).then_inc(q0_left, 1)
            dve.wait_ge(q0_left, 1)
            dve.tensor_copy(q_hi[:, 0:QH], qf[:, 0:QH]).then_inc(q0_left, 1)
            make_p23(1)
            dve.wait_ge(q0_left, 2)
            dve.tensor_tensor(q_lo[:, 0:QH], qf[:, 0:QH], q_hi[:, 0:QH], ALU.subtract).then_inc(q0_left_lo, 1)
            make_p_lo(0, 0, 1)
            make_p_lo(0, 1, 2)
            with dve.Fori(1, S) as i:
                make_ratios(2 * i - 2, 0)
                make_p_lo(i, 0, 2)
                make_ratios(2 * i - 1, 1)
            STEPS = GROUPS * TILES
            with dve.Fori(TILES - 2, STEPS - 3, 2) as step:
                make_ratios(step, 0)
                make_ratios(step + 1, 1)
            make_ratios(STEPS - 2, 0)
            make_ratios(STEPS - 1, 2)
            dve.wait_ge(v0f_made, 1)
            dve.wait_ge(summed, GROUPS - 1)
            for k in range(KC):
                dve.wait_ge(joined_ready, (GROUPS - 1) * KC + k + 1)
                for a in range(AG):
                    if a:
                        dve.wait_ge(added, k * AG + a)
                    dve.scalar_tensor_tensor(acc[:, k, :], joined[k][:, a * CLASSES:(a + 1) * CLASSES],
                                             v0f[:, k, S - AG + a:S - AG + a + 1], acc[:, k, :],
                                             ALU.mult, ALU.add).then_inc(added, 1)

        @block.tensor
        def _(pe):
            pe.wait_ge(ident_set, 2)
            pe.wait_ge(soft, 1)
            for k in range(KC):
                last = pe.transpose(v1_psum[0:S, k * LANES:(k + 1) * LANES], vk[:, k, 1, :], ident[:, :])
            last.then_inc(v1_turned, 1)
            for k in range(KC):
                last = pe.transpose(v1_first[:, k * LANES:(k + 1) * LANES],
                                    vk[:, k, 1, 0:1].broadcast_to([LANES, LANES]), ident[:, :])
            last.then_inc(v1_first_made, 1)

            def turn_p23(h):
                pe.wait_ge(p23_made, h + 1)
                for k in range(KC):
                    last = pe.transpose(turned[h][:, k * LANES:(k + 1) * LANES],
                                        p23[:, k, h * HALF:(h + 1) * HALF], ident[:, :])
                last.then_inc(p23_turned, 1)

            def count_parts(g, tile, k):
                hi = p_hi[:, bass.ds(tile * TW + k * LANES, LANES)]
                lo = p_lo[:, bass.ds(tile * TW + k * LANES, LANES)]
                qh = q_hi[:, bass.ds(g * QW + k * NW, NW)]
                ql = q_lo[:, bass.ds(g * QW + k * NW, NW)]
                return hi, lo, qh, ql

            def count(g, tile, slot):
                out = numbers[slot][:, 0:NW]
                for k in range(KC):
                    hi, lo, qh, ql = count_parts(g, tile, k)
                    pe.matmul(out, hi, qh, start=(k == 0), stop=False)
                    pe.matmul(out, hi, ql, start=False, stop=False)
                    last = pe.matmul(out, lo, qh, start=False, stop=(k == KC - 1))
                last.then_inc(numbers_ready, 1)

            def join_chunk(tile, slot, k, first, final):
                hi = pt_hi[:, bass.ds(tile * TW + k * LANES, LANES)]
                lo = pt_lo[:, bass.ds(tile * TW + k * LANES, LANES)]
                out = joined[k][:, 0:PW]
                pe.matmul(out, hi, r_hi[:, slot, :], start=first, stop=False)
                pe.matmul(out, hi, r_lo[:, slot, :], start=False, stop=False)
                last = pe.matmul(out, lo, r_hi[:, slot, :], start=False, stop=final)
                if final:
                    last.then_inc(joined_ready, 1)

            def join(g, tile, slot, first=False, final=False, freed=None):
                pe.wait_ge(ratios_ready, g * TILES + tile + 1)
                for k in range(KC):
                    if freed is not None:
                        pe.wait_ge(left_made, freed + (k + 1))
                    join_chunk(tile, slot, k, first, final)

            out = numbers[0][:, 0:NW]
            turn_p23(0)
            pe.wait_ge(p_hi_made, 1)
            for k in range(KC):
                if k == 0:
                    pe.wait_ge(q0_left, 2)
                if k == KC // 2:
                    turn_p23(1)
                    pe.wait_ge(q0_right_hi, 1)
                hi, lo, qh, ql = count_parts(0, 0, k)
                pe.matmul(out, hi, qh, start=(k == 0), stop=False)
            for k in range(KC // 2):
                if k == 0:
                    pe.wait_ge(q0_left_lo, 1)
                hi, lo, qh, ql = count_parts(0, 0, k)
                pe.matmul(out, hi, ql, start=False, stop=False)
            for k in range(KC):
                if k == 0:
                    pe.wait_ge(p_ready, 1)
                hi, lo, qh, ql = count_parts(0, 0, k)
                pe.matmul(out, lo, qh, start=False, stop=False)
            for k in range(KC // 2, KC):
                if k == KC // 2:
                    pe.wait_ge(q0_right_lo, 1)
                hi, lo, qh, ql = count_parts(0, 0, k)
                last = pe.matmul(out, hi, ql, start=False, stop=(k == KC - 1))
            last.then_inc(numbers_ready, 1)
            pe.wait_ge(p_ready, 2)
            count(0, 1, 1)
            pe.wait_ge(pt_ready, 1)
            pe.wait_ge(v1_first_copied, 1)
            pe.wait_ge(v1_copied, 1)
            join(0, 0, 0, first=True)

            def middle(g, end, make=False):
                with pe.Fori(1, end) as i:
                    if make:
                        pe.wait_ge(p_ready, 2 * i + 2)
                    count(g, 2 * i, 0)
                    if make:
                        pe.wait_ge(pt_ready, 2 * i)
                    join(g, 2 * i - 1, 1)
                    count(g, 2 * i + 1, 1)
                    if make:
                        pe.wait_ge(pt_ready, 2 * i + 1)
                    join(g, 2 * i, 0)

            def turn_of_group(g):
                pe.wait_ge(q_ready, g)
                count(g, 0, 0)
                join(g - 1, TILES - 1, 1, final=True)
                count(g, 1, 1)
                join(g, 0, 0, first=True, freed=(g - 1) * KC)

            middle(0, S, make=True)
            pe.wait_ge(pt_ready, TILES)
            with pe.Fori(1, GROUPS - 1) as g:
                turn_of_group(g)
                middle(g, S)
            g = GROUPS - 1
            turn_of_group(g)
            middle(g, S - 1)
            count(g, TILES - 2, 0)
            count(g, TILES - 1, 2)
            join(g, TILES - 3, 1)
            pe.wait_ge(ratios_ready, g * TILES + TILES)
            for k in range(KC):
                join_chunk(TILES - 2, 0, k, False, False)
                join_chunk(TILES - 1, 2, k, False, True)


_INS = ["r_logits", "r_y_true"]
_OUTS = [((512, 100), "float32")]


def kernel(**inputs):
    import numpy as _np
    import concourse.bacc as _bacc
    from concourse import mybir as _mybir
    from concourse.bass_utils import run_bass_kernel_spmd as _run

    nc = _bacc.Bacc("TRN2", target_bir_lowering=False, num_devices=1)
    arrays, args = {}, []
    for name in _INS:
        a = _np.ascontiguousarray(inputs[name])
        arrays[f"in_{name}_dram"] = a
        args.append(nc.dram_tensor(f"in_{name}_dram", a.shape, _mybir.dt.from_np(a.dtype), kind="ExternalInput").ap())
    for i, (shape, dtype) in enumerate(_OUTS):
        dt = _mybir.dt.from_np(_np.dtype(dtype))
        args.append(nc.dram_tensor(f"out_{i}_dram", shape, dt, kind="ExternalOutput").ap())
    joint_classifier(nc, *args)
    r = _run(nc, [arrays], core_ids=[0])
    return r.results[0]["out_0_dram"]
```
